# Optimizing a Trainium2 kernel written in Bass

```python
import numpy as np
import jax
import jax.numpy as jnp

def _softmax(x, axis=-1):
    return jax.nn.softmax(x, axis=axis)

def _gelu(x):
    return jax.nn.gelu(x, approximate=True)

def _silu(x):
    return jax.nn.silu(x)

def _sigmoid(x):
    return jax.nn.sigmoid(x)

def _layernorm(x, axis=-1, eps=1e-05):
    m = jnp.mean(x, axis=axis, keepdims=True)
    v = jnp.var(x, axis=axis, keepdims=True)
    return (x - m) / jnp.sqrt(v + eps)

def _scatter_add(tgt, idx, src, axis=0):
    return tgt.at[idx].add(src)

def _segment_sum(src, seg, n):
    return jax.ops.segment_sum(src, seg, n)
kernel_name = 'mk_sandwich_d1_jaxref_r8_12d6d6'

def setup_inputs(seed: int=0):
    np.random.seed(seed)
    _w = jnp.asarray

    def _L0_attn_setup():
        import jax, jax.numpy as jnp
        import numpy as np
        from jax import lax
        D_MODEL = 128
        LN_EPS = 1e-05

        def _layer_norm(x, gamma, beta):
            mu = jnp.mean(x, axis=-1, keepdims=True)
            var = jnp.mean(jnp.square(x - mu), axis=-1, keepdims=True)
            return (x - mu) * lax.rsqrt(var + LN_EPS) * gamma + beta
        key = jax.random.key(seed)
        ks = jax.random.split(key, 9)
        B, L, D = (2, 256, D_MODEL)
        x = jax.random.normal(ks[0], (B, L, D), dtype=jnp.float32)
        A_param = jax.random.normal(ks[1], (D,), dtype=jnp.float32) * 0.1
        B_vec = jax.random.normal(ks[2], (D,), dtype=jnp.float32)
        C_vec = jax.random.normal(ks[3], (D,), dtype=jnp.float32)
        D_vec = jax.random.normal(ks[4], (D,), dtype=jnp.float32)
        W_proj = jax.random.normal(ks[5], (D, D), dtype=jnp.float32) * (1.0 / np.sqrt(D))
        b_proj = jax.random.normal(ks[6], (D,), dtype=jnp.float32) * 0.01
        gamma = jnp.ones((D,), dtype=jnp.float32)
        beta = jnp.zeros((D,), dtype=jnp.float32)
        return {'x': x, 'A_param': A_param, 'B_vec': B_vec, 'C_vec': C_vec, 'D_vec': D_vec, 'W_proj': W_proj, 'b_proj': b_proj, 'gamma': gamma, 'beta': beta}
    _L0_attn_in = _L0_attn_setup()

    def _L0_ffn_setup():
        import jax, jax.numpy as jnp
        import numpy as np
        DIM = 128

        def _reference_tuple_inner(x, W_r, W_k, W_v, mu_r, mu_k):
            B, T, C = x.shape
            x_prev = jnp.concatenate([jnp.zeros((B, 1, C), x.dtype), x[:, :-1, :]], axis=1)
            xr = mu_r * x + (1.0 - mu_r) * x_prev
            xk = mu_k * x + (1.0 - mu_k) * x_prev
            r = jax.nn.sigmoid(jnp.einsum('btc,dc->btd', xr, W_r))
            k = jnp.einsum('btc,dc->btd', xk, W_k)
            k_act = jnp.square(jax.nn.relu(k))
            out = r * jnp.einsum('btc,dc->btd', k_act, W_v)
            new_state = x[:, -1, :]
            return (out, new_state)
        key = jax.random.key(seed)
        ks = jax.random.split(key, 6)
        B, T, C = (8, 256, DIM)
        x = jax.random.normal(ks[0], (B, T, C), dtype=jnp.float32)
        s = 1.0 / np.sqrt(C)
        W_r = jax.random.uniform(ks[1], (C, C), jnp.float32, -s, s)
        W_k = jax.random.uniform(ks[2], (C, C), jnp.float32, -s, s)
        W_v = jax.random.uniform(ks[3], (C, C), jnp.float32, -s, s)
        mu_r = jax.random.uniform(ks[4], (C,), jnp.float32)
        mu_k = jax.random.uniform(ks[5], (C,), jnp.float32)
        return {'x': x, 'W_r': W_r, 'W_k': W_k, 'W_v': W_v, 'mu_r': mu_r, 'mu_k': mu_k}
    _L0_ffn_in = _L0_ffn_setup()
    _d = {'L0_attn_x': _L0_attn_in['x'], 'L0_attn_A_param': _L0_attn_in['A_param'], 'L0_attn_B_vec': _L0_attn_in['B_vec'], 'L0_attn_C_vec': _L0_attn_in['C_vec'], 'L0_attn_D_vec': _L0_attn_in['D_vec'], 'L0_attn_W_proj': _L0_attn_in['W_proj'], 'L0_attn_b_proj': _L0_attn_in['b_proj'], 'L0_attn_gamma': _L0_attn_in['gamma'], 'L0_attn_beta': _L0_attn_in['beta'], 'L0_ffn_W_r': _L0_ffn_in['W_r'], 'L0_ffn_W_k': _L0_ffn_in['W_k'], 'L0_ffn_W_v': _L0_ffn_in['W_v'], 'L0_ffn_mu_r': _L0_ffn_in['mu_r'], 'L0_ffn_mu_k': _L0_ffn_in['mu_k']}
    _x0 = _d['L0_attn_x']
    _d['L0_attn_x'] = jax.random.normal(jax.random.fold_in(jax.random.key(seed), 1), (32, 256, 128), dtype=_x0.dtype)
    del _x0
    return _d

def reference(L0_attn_x, L0_attn_A_param, L0_attn_B_vec, L0_attn_C_vec, L0_attn_D_vec, L0_attn_W_proj, L0_attn_b_proj, L0_attn_gamma, L0_attn_beta, L0_ffn_W_r, L0_ffn_W_k, L0_ffn_W_v, L0_ffn_mu_r, L0_ffn_mu_k):

    def _L0_attn_ref(x, A_param, B_vec, C_vec, D_vec, W_proj, b_proj, gamma, beta):
        import jax, jax.numpy as jnp
        import numpy as np
        from jax import lax
        D_MODEL = 128
        LN_EPS = 1e-05

        def _layer_norm(x, gamma, beta):
            mu = jnp.mean(x, axis=-1, keepdims=True)
            var = jnp.mean(jnp.square(x - mu), axis=-1, keepdims=True)
            return (x - mu) * lax.rsqrt(var + LN_EPS) * gamma + beta
        Bsz, L, D = x.shape
        A = jax.nn.sigmoid(A_param)
        t = jnp.arange(L, dtype=jnp.float32)
        A_t = A[:, None] ** t[None, :]
        K = (C_vec[:, None] * A_t * B_vec[:, None])[:, None, :]
        x_t = jnp.transpose(x, (0, 2, 1))
        out = lax.conv_general_dilated(x_t, K, window_strides=(1,), padding=[(L - 1, L - 1)], dimension_numbers=('NCH', 'OIH', 'NCH'), feature_group_count=D)
        out = out[..., :L] + D_vec[None, :, None] * x_t
        out = jnp.transpose(out, (0, 2, 1))
        out = jnp.dot(jax.nn.gelu(out, approximate=False), W_proj.T) + b_proj
        return _layer_norm(x + out, gamma, beta)

    def _L0_ffn_ref(x, W_r, W_k, W_v, mu_r, mu_k):
        import jax, jax.numpy as jnp
        import numpy as np
        DIM = 128

        def _reference_tuple_inner(x, W_r, W_k, W_v, mu_r, mu_k):
            B, T, C = x.shape
            x_prev = jnp.concatenate([jnp.zeros((B, 1, C), x.dtype), x[:, :-1, :]], axis=1)
            xr = mu_r * x + (1.0 - mu_r) * x_prev
            xk = mu_k * x + (1.0 - mu_k) * x_prev
            r = jax.nn.sigmoid(jnp.einsum('btc,dc->btd', xr, W_r))
            k = jnp.einsum('btc,dc->btd', xk, W_k)
            k_act = jnp.square(jax.nn.relu(k))
            out = r * jnp.einsum('btc,dc->btd', k_act, W_v)
            new_state = x[:, -1, :]
            return (out, new_state)
        return _reference_tuple_inner(x, W_r, W_k, W_v, mu_r, mu_k)[0]
    x = L0_attn_x
    x = x + _layernorm(_L0_attn_ref(_layernorm(x, axis=-1), L0_attn_A_param, L0_attn_B_vec, L0_attn_C_vec, L0_attn_D_vec, L0_attn_W_proj, L0_attn_b_proj, L0_attn_gamma, L0_attn_beta), axis=-1)
    x = x + _layernorm(_L0_ffn_ref(_layernorm(x, axis=-1), L0_ffn_W_r, L0_ffn_W_k, L0_ffn_W_v, L0_ffn_mu_r, L0_ffn_mu_k), axis=-1)
    return x

_drawn_inputs = setup_inputs


def setup_inputs(seed=0):
    import zlib

    import numpy as np

    out = dict(_drawn_inputs(seed))
    spreads = {'L0_attn_gamma': (1.0, 0.2), 'L0_attn_beta': (0.0, 0.1)}
    factors = {'L0_attn_A_param': 8.0,
     'L0_attn_B_vec': 2.918,
     'L0_attn_C_vec': 2.971,
     'L0_attn_b_proj': 8.0}
    for name, (base, spread) in spreads.items():
        noise = np.random.default_rng([zlib.crc32(name.encode()), seed]).standard_normal(out[name].shape)
        drawn = base * np.exp(spread * noise) if base else spread * noise
        out[name] = jnp.asarray(drawn.astype(out[name].dtype))
    for name, factor in factors.items():
        out[name] = (out[name] * factor).astype(out[name].dtype)
    return out
```

```python
import concourse.bass as bass
from concourse import mybir
from contextlib import ExitStack

P = 128
SEQ = 256
HALF = 4
TILES = 2 * HALF
HW = HALF * P
GW = TILES * P
EPS = 1e-5


def sandwich(nc, x, A_param, B_vec, C_vec, D_vec, W_proj, b_proj, gamma, beta, W_r, W_k, W_v, mu_r, mu_k, out):
    fp32 = mybir.dt.float32
    ALU = mybir.AluOpType
    ACT = mybir.ActivationFunctionType
    AX = mybir.AxisListType.X

    tokens = x.shape[0] * x.shape[1]
    GROUPS = tokens // GW
    LAST = GROUPS - 1
    x_dram = x.rearrange("b l c -> (b l) c").rearrange("(n p) c -> p n c", p=P)
    out_dram = out.rearrange("b l c -> (b l) c").rearrange("(n p) c -> p n c", p=P)

    def column(v):
        return v.rearrange("(p a) -> p a", a=1)

    ctx = ExitStack()
    with ctx:
        def sb(name, *shape):
            return ctx.enter_context(nc.sbuf_tensor(name, [P, *shape], fp32))

        def pb(name):
            return ctx.enter_context(nc.psum_tensor(name, [P, HW], fp32))

        def sem(name):
            return ctx.enter_context(nc.semaphore(name))

        ident = sb("ident", P)
        prefix_ones = sb("prefix_ones", SEQ)
        neg_half = sb("neg_half", TILES)
        eps_tile = sb("eps_tile", TILES)
        a_col = sb("a_col", 1)
        b_col = sb("b_col", 1)
        c_col = sb("c_col", 1)
        d_col = sb("d_col", 1)
        bias_col = sb("bias_col", 1)
        bias_row = sb("bias_row", P)
        gamma_row = sb("gamma_row", P)
        beta_row = sb("beta_row", P)
        mu_rows = sb("mu_rows", 2, P)
        w_rk = sb("w_rk", 2, P)
        w_pv = sb("w_pv", 2, P)
        a_pow = sb("a_pow", 1, 8)
        pow_up = sb("pow_up", SEQ)
        pow_down = sb("pow_down", SEQ)
        pow_token = sb("pow_token", 2, P)
        mixed = sb("mixed", 4, P)
        mixed_T = sb("mixed_T", 4, P)
        pv_T = sb("pv_T", 2, P)
        sums = sb("sums", 8)

        x_all = sb("x_all", GROUPS * GW)

        xn = [sb(f"xn{h}", HW) for h in range(2)]
        xn_pow = [sb(f"xn_pow{h}", HW) for h in range(2)]
        xnT = [sb(f"xnT{h}", HW) for h in range(2)]
        conv_scaled = [sb(f"conv_scaled{h}", HW) for h in range(2)]
        conv = [sb(f"conv{h}", HW) for h in range(2)]
        gelu = [sb(f"gelu{h}", HW) for h in range(2)]
        y = [sb(f"y{h}", HW) for h in range(2)]
        ts_ = [sb(f"t_scaled{h}", HW) for h in range(2)]
        tsT = [sb(f"tsT{h}", 2, SEQ + 1) for h in range(2)]
        k_act = [sb(f"k_act{h}", HW) for h in range(2)]
        tanh = [sb(f"tanh{h}", HW) for h in range(2)]
        f = [sb(f"f{h}", HW) for h in range(2)]
        junk = sb("junk", GW)

        def stats(name):
            return {"raw": sb(f"{name}_raw", TILES, 6),
                    **{k: sb(f"{name}_{k}", TILES) for k in ("diff", "m2", "sq", "msum", "negmean", "ve", "r")}}

        Sx, Sy, St, Sf = (stats(n) for n in ("sx", "sy", "st", "sf"))
        z_var = sb("z_var", TILES)
        z_ve = sb("z_ve", TILES)
        z_r = sb("z_r", TILES)
        x_bias = sb("x_bias", TILES)
        y_shift = sb("y_shift", TILES)
        t_shift = sb("t_shift", TILES)
        f_shift = sb("f_shift", TILES)
        out_bias = sb("out_bias", TILES)

        ps_xT, ps_prefix, ps_z0, ps_z1, ps_tT, ps_k, ps_r, ps_v = (
            pb(n) for n in ("ps_xT", "ps_prefix", "ps_z0", "ps_z1", "ps_tT", "ps_k", "ps_r", "ps_v"))
        ps_z = [ps_z0, ps_z1]

        s_vecs, s_rows, s_wts = sem("vecs_loaded"), sem("rows_loaded"), sem("weights_loaded")
        s_const, s_A, s_pow, s_chain = sem("constants"), sem("A_ready"), sem("powers_ready"), sem("setup_chain")
        s_mixed, s_setupT, s_ready = sem("mixed_ready"), sem("setup_transposed"), sem("weights_ready")
        s_bias, s_filled = sem("bias_ready"), sem("filled")
        s_x0, s_x1, s_xrest = sem("x0_loaded"), sem("x1_loaded"), sem("x_rest_loaded")
        x_stats, x_moments, x_scale = sem("x_stats"), sem("x_moments"), sem("x_scale")
        xn_ready, xn_pow_ready, xT_ready, xT_copied = (sem(n) for n in (
            "xn_ready", "xn_pow_ready", "xT_ready", "xT_copied"))
        prefix_ready, scaled_ready, conv_ready, gelu_ready = (sem(n) for n in (
            "prefix_ready", "scaled_ready", "conv_ready", "gelu_ready"))
        z_ready, y_scaled, y_ready = sem("z_ready"), sem("y_scaled"), sem("y_ready")
        z_squares, z_scale = sem("z_squares"), sem("z_scale")
        y_stats, y_moments, y_scale, t_ready = (sem(n) for n in ("y_stats", "y_moments", "y_scale", "t_ready"))
        t_stats, t_moments, t_scale = sem("t_stats"), sem("t_moments"), sem("t_scale")
        ts_ready, tT_ready, tT_copied = sem("ts_ready"), sem("tT_ready"), sem("tT_copied")
        k_ready, r_ready, relu_done, k_act_ready, tanh_done, v_ready, f_ready = (sem(n) for n in (
            "k_ready", "r_ready", "relu_done", "k_act_ready", "tanh_done", "v_ready", "f_ready"))
        f_stats, f_moments, f_scale = sem("f_stats"), sem("f_moments"), sem("f_scale")
        out_partial, out_ready, stored = sem("out_partial"), sem("out_ready"), sem("stored")
        pc = {n: sem(f"pool_{n}") for n in ("x", "z", "y", "t", "f", "f_shift")}
        dc = {n: (sem(f"dve_{n}_diff"), sem(f"dve_{n}_sq")) for n in ("x", "y", "t", "f")}

        block = ctx.enter_context(nc.Block())

        def tile(t, j):
            return t[:, j * P:(j + 1) * P]

        def xa(g, j, n=1):
            return x_all[:, bass.ds(g * GW + j * P, n * P)]

        def later(eng, s, value, g):
            if not isinstance(g, int) or value > 0:
                eng.wait_ge(s, value)

        @block.sync
        def _(sp):
            sp.dma_start(x_all[:, 0:GW].rearrange("p (n c) -> p n c", c=P), x_dram[:, 0:TILES, :]).then_inc(s_x0, 16)
            sp.dma_start(x_all[:, GW:2 * GW].rearrange("p (n c) -> p n c", c=P),
                         x_dram[:, TILES:2 * TILES, :]).then_inc(s_x1, 16)
            with sp.Fori(2, GROUPS) as g:
                sp.dma_start(x_all[:, bass.ds(g * GW, GW)].rearrange("p (n c) -> p n c", c=P),
                             x_dram[:, bass.ds(g * TILES, TILES), :]).then_inc(s_xrest, 16)
            with sp.Fori(0, GROUPS) as g:
                sp.wait_ge(out_ready, g + 1)
                sp.dma_start(out_dram[:, bass.ds(g * TILES, TILES), :],
                             x_all[:, bass.ds(g * GW, GW)].rearrange("p (n c) -> p n c", c=P)).then_inc(stored, 16)
            sp.wait_ge(stored, 16 * GROUPS)

        @block.gpsimd
        def _(pool):
            g_ = nc.gpsimd
            g_.memset(ident[:], 0.0).then_inc(s_filled, 1)
            g_.memset(prefix_ones[:], 1.0).then_inc(s_filled, 1)
            g_.memset(neg_half[:], -0.5)
            g_.memset(eps_tile[:], EPS)
            for h in range(2):
                g_.memset(tsT[h][:, :, 0:1], 0.0)
            pool.wait_ge(s_filled, 2)
            g_.affine_select(out=ident[:], in_=ident[:], compare_op=ALU.not_equal, fill=1.0, base=0,
                             pattern=[[-1, P]], channel_multiplier=1)
            g_.affine_select(out=prefix_ones[:], in_=prefix_ones[:], compare_op=ALU.is_ge, fill=0.0, base=0,
                             pattern=[[1, SEQ]], channel_multiplier=-1).then_inc(s_const, 1)

            def inverse_std(s, done, g):
                g_.tensor_tensor(s["r"][:], s["ve"][:], neg_half[:], ALU.pow).then_inc(done, 1)
                g_.tensor_scalar(s["negmean"][:], s["msum"][:], -0.5, None, ALU.mult).then_inc(done, 1)
                pool.wait_ge(done, 2 * g + 2)

            def pre_scale(g):
                pool.wait_ge(x_moments, g + 1)
                later(pool, xn_ready, 2 * g, g)
                inverse_std(Sx, pc["x"], g)
                g_.tensor_tensor(x_bias[:], Sx["negmean"][:], Sx["r"][:], ALU.mult).then_inc(x_scale, 1)

            def xn_times_pow(g, h):
                n = 2 * g + h
                pool.wait_ge(xn_ready, n + 1)
                later(pool, prefix_ready, n - 1, g)
                g_.tensor_tensor(xn_pow[h][:].rearrange("p (q l) -> p q l", l=SEQ),
                                 xn[h][:].rearrange("p (q l) -> p q l", l=SEQ),
                                 pow_token[:].rearrange("p j c -> p (j c)")[:, None, :].to_broadcast([P, 2, SEQ]),
                                 ALU.mult).then_inc(xn_pow_ready, 1)

            def z_scale_of(g):
                pool.wait_ge(z_squares, g + 1)
                later(pool, y_scaled, 2 * g, g)
                g_.tensor_tensor(z_ve[:], z_var[:], eps_tile[:], ALU.add).then_inc(pc["z"], 1)
                pool.wait_ge(pc["z"], g + 1)
                g_.tensor_tensor(z_r[:], z_ve[:], neg_half[:], ALU.pow).then_inc(z_scale, 1)

            def add_beta(g, h):
                pool.wait_ge(y_scaled, 2 * g + h + 1)
                yv = y[h][:].rearrange("p (j c) -> p j c", c=P)
                g_.tensor_tensor(yv, yv, beta_row[:, None, :].to_broadcast([P, HALF, P]), ALU.add).then_inc(y_ready, 1)

            def y_scale_of(g):
                pool.wait_ge(y_moments, g + 1)
                later(pool, t_ready, g, g)
                inverse_std(Sy, pc["y"], g)
                g_.tensor_tensor(y_shift[:], Sy["negmean"][:], Sy["r"][:], ALU.mult).then_inc(y_scale, 1)

            def t_scale_of(g):
                pool.wait_ge(t_moments, g + 1)
                later(pool, ts_ready, 2 * g, g)
                g_.tensor_tensor(St["r"][:], St["ve"][:], neg_half[:], ALU.pow).then_inc(t_scale, 1)
                g_.tensor_copy(t_shift[:], y_shift[:]).then_inc(pc["t"], 1)

            def f_scale_of(g):
                pool.wait_ge(f_moments, g + 1)
                inverse_std(Sf, pc["f"], g)
                g_.tensor_tensor(f_shift[:], Sf["negmean"][:], Sf["r"][:], ALU.mult).then_inc(pc["f_shift"], 1)
                later(pool, out_ready, g, g)
                pool.wait_ge(pc["t"], g + 1)
                pool.wait_ge(pc["f_shift"], g + 1)
                g_.tensor_tensor(out_bias[:], f_shift[:], t_shift[:], ALU.add).then_inc(f_scale, 1)

            def body(g, pre=True, mid=True, back=True):
                if back:
                    t_scale_of(g - 1)
                if mid:
                    z_scale_of(g)
                if pre:
                    pre_scale(g + 1)
                if mid:
                    add_beta(g, 0)
                    add_beta(g, 1)
                if pre:
                    xn_times_pow(g + 1, 0)
                if mid:
                    y_scale_of(g)
                if pre:
                    xn_times_pow(g + 1, 1)
                if back:
                    f_scale_of(g - 1)

            pool.wait_ge(s_const, 1)
            pre_scale(0)
            pool.wait_ge(s_pow, 1)
            xn_times_pow(0, 0)
            xn_times_pow(0, 1)
            pool.wait_ge(s_rows, 16 * 5)
            body(0, back=False)
            body(1)
            with pool.Fori(2, LAST) as g:
                body(g)
            body(LAST, pre=False)
            body(GROUPS, pre=False, mid=False)

        @block.scalar
        def _(act):
            a_ = nc.scalar
            for dst, src in ((a_col, A_param), (b_col, B_vec), (c_col, C_vec), (d_col, D_vec), (bias_col, b_proj)):
                act.dma_start(dst[:], column(src)).then_inc(s_vecs, 16)
            for i, w in enumerate((W_proj, W_v)):
                act.dma_start(w_pv[:, i, :], w).then_inc(s_wts, 16)
            for i, w in enumerate((W_r, W_k)):
                act.dma_start(w_rk[:, i, :], w).then_inc(s_wts, 16)
            for dst, src in ((mu_rows[:, 0, :], mu_r), (mu_rows[:, 1, :], mu_k), (bias_row[:], b_proj),
                             (gamma_row[:], gamma), (beta_row[:], beta)):
                act.dma_start(dst, src.partition_broadcast(P)).then_inc(s_rows, 16)
            act.wait_ge(s_vecs, 16 * 5)
            a_.activation(a_pow[:, 0, 0:1], a_col[:], ACT.Sigmoid).then_inc(s_A, 1)

            def normalise(g, h):
                n = 2 * g + h
                act.wait_ge(x_scale, g + 1)
                later(act, xT_ready, n - 1, g)
                later(act, xn_pow_ready, n - 1, g)
                for j in range(HALF):
                    k = h * HALF + j
                    last = a_.activation(tile(xn[h], j), xa(g, k), ACT.Identity, bias=x_bias[:, k:k + 1],
                                         scale=Sx["r"][:, k:k + 1])
                last.then_inc(xn_ready, 1)

            def copy_xT(g, h):
                n = 2 * g + h
                act.wait_ge(xT_ready, n + 1)
                later(act, z_ready, n - 1, g)
                a_.activation(xnT[h][:], ps_xT[:], ACT.Identity, bias=bias_col[:]).then_inc(xT_copied, 1)

            def gelu_of(g, h):
                n = 2 * g + h
                act.wait_ge(conv_ready, n + 1)
                later(act, z_ready, n - 1, g)
                a_.activation(gelu[h][:], conv[h][:], ACT.Gelu).then_inc(gelu_ready, 1)

            def square_z(g):
                later(act, z_scale, g, g)
                for h in range(2):
                    act.wait_ge(z_ready, 2 * g + h + 1)
                    for j in range(HALF):
                        k = h * HALF + j
                        last = a_.activation(tile(junk, k), tile(ps_z[h], j), ACT.Square, scale=float(P) ** -0.5,
                                             accum_out=z_var[:, k:k + 1])
                last.then_inc(z_squares, 1)

            def finish(g):
                act.wait_ge(out_partial, g + 1)
                for k in range(TILES):
                    last = a_.activation(xa(g, k), xa(g, k), ACT.Identity, bias=out_bias[:, k:k + 1])
                last.then_inc(out_ready, 1)

            def copy_tT(g, h):
                n = 2 * g + h
                act.wait_ge(tT_ready, n + 1)
                later(act, r_ready, n - 1, g)
                a_.activation(tsT[h][:, :, 1:SEQ + 1], ps_tT[:].rearrange("p (q l) -> p q l", l=SEQ),
                              ACT.Copy).then_inc(tT_copied, 1)

            def relu_k(g, h):
                n = 2 * g + h
                act.wait_ge(k_ready, n + 1)
                later(act, v_ready, n - 1, g)
                a_.activation(k_act[h][:], ps_k[:], ACT.Relu).then_inc(relu_done, 1)

            def square_k(g, h):
                act.wait_ge(relu_done, 2 * g + h + 1)
                a_.activation(k_act[h][:], k_act[h][:], ACT.Square).then_inc(k_act_ready, 1)

            def tanh_r(g, h):
                n = 2 * g + h
                act.wait_ge(r_ready, n + 1)
                later(act, f_ready, n - 1, g)
                a_.activation(tanh[h][:], ps_r[:], ACT.Tanh, scale=0.5).then_inc(tanh_done, 1)

            def body(g, pre=True, mid=True, back=True, post=True):
                if mid:
                    copy_xT(g, 0)
                    gelu_of(g, 0)
                    copy_xT(g, 1)
                    gelu_of(g, 1)
                if post:
                    finish(g - 2)
                if mid:
                    square_z(g)
                if back:
                    copy_tT(g - 1, 0)
                    copy_tT(g - 1, 1)
                if pre:
                    normalise(g + 1, 0)
                if back:
                    relu_k(g - 1, 0)
                    tanh_r(g - 1, 0)
                    square_k(g - 1, 0)
                if pre:
                    normalise(g + 1, 1)
                if back:
                    relu_k(g - 1, 1)
                    tanh_r(g - 1, 1)
                    square_k(g - 1, 1)

            normalise(0, 0)
            normalise(0, 1)
            act.wait_ge(s_bias, 1)
            body(0, back=False, post=False)
            body(1, post=False)
            with act.Fori(2, LAST) as g:
                body(g)
            body(LAST, pre=False)
            body(GROUPS, pre=False, mid=False)
            finish(LAST)

        @block.vector
        def _(dve):
            v_ = nc.vector
            link_count = [0]

            def link(ins):
                link_count[0] += 1
                ins.then_inc(s_chain, 1)
                dve.wait_ge(s_chain, link_count[0])

            def moments(s, name, g, source, stats_done, moments_done, used, ready=None):
                for k in range(TILES):
                    if ready is not None and k % HALF == 0:
                        dve.wait_ge(ready, 2 * g + k // HALF + 1)
                    last = v_.bn_stats(s["raw"][:, k, :], source(k))
                last.then_inc(stats_done, 1)
                join(s, name, g, stats_done, moments_done, used)

            def join(s, name, g, stats_done, moments_done, used, eps=EPS):
                even_mean, even_m2, odd_mean, odd_m2 = (s["raw"][:, :, c] for c in (1, 2, 4, 5))
                dve.wait_ge(stats_done, g + 1)
                later(dve, used, g, g)
                v_.tensor_tensor(s["diff"][:], even_mean, odd_mean, ALU.subtract).then_inc(dc[name][0], 1)
                v_.tensor_tensor(s["msum"][:], even_mean, odd_mean, ALU.add)
                v_.scalar_tensor_tensor(s["m2"][:], even_m2, P * eps, odd_m2, ALU.add, ALU.add)
                dve.wait_ge(dc[name][0], g + 1)
                v_.scalar_tensor_tensor(s["sq"][:], s["diff"][:], 0.25, s["diff"][:], ALU.mult,
                                        ALU.mult).then_inc(dc[name][1], 1)
                dve.wait_ge(dc[name][1], g + 1)
                v_.scalar_tensor_tensor(s["ve"][:], s["m2"][:], 1.0 / P, s["sq"][:], ALU.mult,
                                        ALU.add).then_inc(moments_done, 1)

            def pre_moments(g):
                if isinstance(g, int) and g < 2:
                    dve.wait_ge((s_x0, s_x1)[g], 16)
                else:
                    dve.wait_ge(s_xrest, 16 * (GROUPS - 2))
                moments(Sx, "x", g, lambda k: xa(g, k), x_stats, x_moments, x_scale)

            def convolve(g, h):
                n = 2 * g + h
                dve.wait_ge(prefix_ready, n + 1)
                v_.tensor_tensor(conv_scaled[h][:].rearrange("p (q l) -> p q l", l=SEQ),
                                 ps_prefix[:].rearrange("p (q l) -> p q l", l=SEQ),
                                 pow_down[:, None, :].to_broadcast([P, 2, SEQ]), ALU.mult).then_inc(scaled_ready, 1)
                dve.wait_ge(scaled_ready, n + 1)
                dve.wait_ge(xT_copied, n + 1)
                later(dve, gelu_ready, n - 1, g)
                v_.scalar_tensor_tensor(conv[h][:], ps_xT[:], d_col[:], conv_scaled[h][:], ALU.mult,
                                        ALU.add).then_inc(conv_ready, 1)

            def scale_z(g, h):
                dve.wait_ge(z_scale, g + 1)
                for j in range(HALF):
                    k = h * HALF + j
                    last = v_.scalar_tensor_tensor(tile(y[h], j), tile(ps_z[h], j), z_r[:, k:k + 1], gamma_row[:],
                                                   ALU.mult, ALU.mult)
                last.then_inc(y_scaled, 1)

            def residual(g):
                dve.wait_ge(y_scale, g + 1)
                for k in range(TILES):
                    last = v_.scalar_tensor_tensor(xa(g, k), tile(y[k // HALF], k % HALF), Sy["r"][:, k:k + 1],
                                                   xa(g, k), ALU.mult, ALU.add)
                last.then_inc(t_ready, 1)

            def scale_t(g, h):
                n = 2 * g + h
                dve.wait_ge(t_scale, g + 1)
                later(dve, tT_ready, n - 1, g)
                v_.tensor_tensor(ts_[h][:].rearrange("p (j c) -> p j c", c=P),
                                 xa(g, h * HALF, HALF).rearrange("p (j c) -> p j c", c=P),
                                 St["r"][:, h * HALF:(h + 1) * HALF, None].to_broadcast([P, HALF, P]),
                                 ALU.mult).then_inc(ts_ready, 1)

            def gate(g, h):
                n = 2 * g + h
                dve.wait_ge(v_ready, n + 1)
                dve.wait_ge(tanh_done, n + 1)
                v_.scalar_tensor_tensor(f[h][:], tanh[h][:], 1.0, ps_v[:], ALU.add, ALU.mult).then_inc(f_ready, 1)

            def gate_stats(g, h):
                dve.wait_ge(f_ready, 2 * g + h + 1)
                for j in range(HALF):
                    last = v_.bn_stats(Sf["raw"][:, h * HALF + j, :], tile(f[h], j))
                if h == 1:
                    last.then_inc(f_stats, 1)
                    join(Sf, "f", g, f_stats, f_moments, f_scale, 4 * EPS)

            def add_f(g):
                dve.wait_ge(f_scale, g + 1)
                for k in range(TILES):
                    last = v_.scalar_tensor_tensor(xa(g, k), tile(f[k // HALF], k % HALF), Sf["r"][:, k:k + 1],
                                                   xa(g, k), ALU.mult, ALU.add)
                last.then_inc(out_partial, 1)

            def body(g, pre=True, mid=True, back=True):
                if mid:
                    convolve(g, 0)
                    convolve(g, 1)
                if back:
                    dve.wait_ge(t_ready, g)
                    moments(St, "t", g - 1, lambda k: xa(g - 1, k), t_stats, t_moments, t_scale)
                if pre:
                    pre_moments(g + 1)
                if back:
                    scale_t(g - 1, 0)
                    scale_t(g - 1, 1)
                if mid:
                    scale_z(g, 0)
                    scale_z(g, 1)
                if back:
                    gate(g - 1, 0)
                    gate_stats(g - 1, 0)
                if mid:
                    moments(Sy, "y", g, lambda k: tile(y[k // HALF], k % HALF), y_stats, y_moments, y_scale, y_ready)
                if back:
                    gate(g - 1, 1)
                    gate_stats(g - 1, 1)
                    add_f(g - 1)
                if mid:
                    residual(g)

            pre_moments(0)
            dve.wait_ge(s_vecs, 16 * 5)
            v_.memset(pow_up[:, 0:1], 1.0)
            link(v_.tensor_tensor(pow_down[:, SEQ - 1:SEQ], c_col[:], b_col[:], ALU.mult))
            dve.wait_ge(s_A, 1)
            for k in range(8):
                n = 1 << k
                power = a_pow[:, 0, k:k + 1]
                v_.tensor_scalar(pow_up[:, n:2 * n], pow_up[:, 0:n], power, None, ALU.mult)
                step = v_.tensor_scalar(pow_down[:, SEQ - 2 * n:SEQ - n], pow_down[:, SEQ - n:SEQ], power, None,
                                        ALU.mult)
                if k < 7:
                    step = v_.tensor_tensor(a_pow[:, 0, k + 1:k + 2], power, power, ALU.mult)
                link(step)
            v_.tensor_copy(sums[:, 7:8], pow_up[:, 0:1]).then_inc(s_mixed, 1)
            dve.wait_ge(s_rows, 16 * 5)
            link(v_.reduce_sum(sums[:, 4:5], bias_row[:], axis=AX))
            link(v_.tensor_scalar(sums[:, 5:6], sums[:, 4:5], 1.0 / P, None, ALU.mult))
            v_.tensor_scalar(bias_col[:], bias_col[:], sums[:, 5:6], None, ALU.subtract).then_inc(s_bias, 1)
            dve.wait_ge(s_wts, 16 * 4)
            mixed_pairs = mixed[:].rearrange("p (w m) c -> p w m c", m=2)
            link(v_.tensor_tensor(mixed_pairs[:, :, 0, :], w_rk[:], mu_rows[:], ALU.mult))
            link(v_.tensor_tensor(mixed_pairs[:, :, 1, :], w_rk[:], mixed_pairs[:, :, 0, :], ALU.subtract))
            link(v_.reduce_sum(sums[:, 0:4], mixed[:], axis=AX))
            link(v_.tensor_scalar(sums[:, 0:4], sums[:, 0:4], 1.0 / P, None, ALU.mult))
            v_.tensor_tensor(mixed[:], mixed[:], sums[:, 0:4, None].to_broadcast([P, 4, P]),
                             ALU.subtract).then_inc(s_mixed, 1)
            dve.wait_ge(s_setupT, 1)
            v_.tensor_copy(pow_token[:].rearrange("p j c -> p (j c)"), ps_v[:, 0:SEQ]).then_inc(s_pow, 1)
            dve.wait_ge(s_setupT, 2)
            link(v_.reduce_sum(sums[:, 4:5], ps_k[:, 0:P], axis=AX))
            link(v_.tensor_scalar(sums[:, 5:6], sums[:, 4:5], 1.0 / P, None, ALU.mult))
            v_.tensor_scalar(pv_T[:, 0, :], ps_k[:, 0:P], sums[:, 5:6], None, ALU.subtract)
            v_.tensor_copy(pv_T[:, 1, :], ps_k[:, P:2 * P])
            dve.wait_ge(s_setupT, 3)
            v_.tensor_copy(mixed_T[:].rearrange("p w c -> p (w c)"), ps_r[:]).then_inc(s_ready, 1)

            body(0, back=False)
            body(1)
            with dve.Fori(2, LAST) as g:
                body(g)
            body(LAST, pre=False)
            body(GROUPS, pre=False, mid=False)

        @block.tensor
        def _(pe):
            t_ = nc.tensor
            pe.wait_ge(s_const, 1)
            pe.wait_ge(s_mixed, 1)
            for j in range(2):
                last = t_.transpose(ps_v[:, j * P:(j + 1) * P], pow_up[:, j * P:(j + 1) * P], ident[:])
            last.then_inc(s_setupT, 1)
            pe.wait_ge(s_wts, 16 * 4)
            for j in range(2):
                last = t_.transpose(ps_k[:, j * P:(j + 1) * P], w_pv[:, j, :], ident[:])
            last.then_inc(s_setupT, 1)
            pe.wait_ge(s_mixed, 2)
            for j in range(4):
                last = t_.transpose(ps_r[:, j * P:(j + 1) * P], mixed[:, j, :], ident[:])
            last.then_inc(s_setupT, 1)

            def transpose_xn(g, h):
                n = 2 * g + h
                pe.wait_ge(xn_ready, n + 1)
                later(pe, conv_ready, n, g)
                for j in range(HALF):
                    last = t_.transpose(tile(ps_xT, j), tile(xn[h], j), ident[:])
                last.then_inc(xT_ready, 1)

            def prefix_sum(g, h):
                n = 2 * g + h
                pe.wait_ge(xn_pow_ready, n + 1)
                later(pe, scaled_ready, n, g)
                for q in range(2):
                    t_.matmul(ps_prefix[:, q * SEQ:(q + 1) * SEQ], tile(xn_pow[h], 2 * q), prefix_ones[:],
                              start=True, stop=False)
                    last = t_.matmul(ps_prefix[:, q * SEQ + P:(q + 1) * SEQ], tile(xn_pow[h], 2 * q + 1),
                                     prefix_ones[:, 0:P], start=False, stop=True)
                last.then_inc(prefix_ready, 1)

            def project(g, h):
                n = 2 * g + h
                pe.wait_ge(gelu_ready, n + 1)
                pe.wait_ge(xT_copied, n + 1)
                later(pe, y_scaled, n - 1, g)
                for j in range(HALF):
                    t_.matmul(tile(ps_z[h], j), tile(gelu[h], j), pv_T[:, 0, :], start=True, stop=False)
                    last = t_.matmul(tile(ps_z[h], j), tile(xnT[h], j), ident[:], is_transpose=True,
                                     start=False, stop=True)
                last.then_inc(z_ready, 1)

            def transpose_t(g, h):
                n = 2 * g + h
                pe.wait_ge(ts_ready, n + 1)
                later(pe, tT_copied, n, g)
                for j in range(HALF):
                    last = t_.transpose(tile(ps_tT, j), tile(ts_[h], j), ident[:])
                last.then_inc(tT_ready, 1)

            def keys(g, h):
                n = 2 * g + h
                pe.wait_ge(tT_copied, n + 1)
                later(pe, relu_done, n, g)
                k_out = ps_k[:].rearrange("p (q l) -> p q l", l=SEQ)
                t_.matmul(k_out, mixed_T[:, 2, :], tsT[h][:, :, 1:SEQ + 1], start=True, stop=False)
                t_.matmul(k_out, mixed_T[:, 3, :], tsT[h][:, :, 0:SEQ], start=False, stop=True).then_inc(k_ready, 1)

            def gates(g, h):
                n = 2 * g + h
                later(pe, tanh_done, n, g)
                for j in range(HALF):
                    q, l = j // 2, (j % 2) * P
                    t_.matmul(tile(ps_r, j), tsT[h][:, q, l + 1:l + 1 + P], mixed_T[:, 0, :], start=True, stop=False)
                    last = t_.matmul(tile(ps_r, j), tsT[h][:, q, l:l + P], mixed_T[:, 1, :], start=False, stop=True)
                last.then_inc(r_ready, 1)

            def values(g, h):
                n = 2 * g + h
                pe.wait_ge(k_act_ready, n + 1)
                later(pe, f_ready, n, g)
                for j in range(HALF):
                    last = t_.matmul(tile(ps_v, j), tile(k_act[h], j), pv_T[:, 1, :], start=True, stop=True)
                last.then_inc(v_ready, 1)

            def body(g, mid=True, back=True):
                if mid:
                    transpose_xn(g, 0)
                    prefix_sum(g, 0)
                    transpose_xn(g, 1)
                    prefix_sum(g, 1)
                    project(g, 0)
                    project(g, 1)
                if back:
                    transpose_t(g - 1, 0)
                    keys(g - 1, 0)
                    transpose_t(g - 1, 1)
                    gates(g - 1, 0)
                    keys(g - 1, 1)
                    gates(g - 1, 1)
                    values(g - 1, 0)
                    values(g - 1, 1)

            pe.wait_ge(s_ready, 1)
            body(0, back=False)
            body(1)
            with pe.Fori(2, GROUPS) as g:
                body(g)
            body(GROUPS, mid=False)


_INS = ["x", "A_param", "B_vec", "C_vec", "D_vec", "W_proj", "b_proj", "gamma", "beta",
        "W_r", "W_k", "W_v", "mu_r", "mu_k"]


def kernel(**inputs):
    import numpy as _np
    import concourse.bacc as _bacc
    from concourse import mybir as _mybir
    from concourse.bass_utils import run_bass_kernel_spmd as _run

    nc = _bacc.Bacc("TRN2", target_bir_lowering=False, num_devices=1)
    arrays, args = {}, []
    for i, name in enumerate(_INS):
        a = _np.ascontiguousarray(inputs[("L0_attn_" if i < 9 else "L0_ffn_") + name])
        arrays[f"in_{name}"] = a
        args.append(nc.dram_tensor(f"in_{name}", a.shape, _mybir.dt.from_np(a.dtype), kind="ExternalInput").ap())
    shape = inputs["L0_attn_x"].shape
    args.append(nc.dram_tensor("out_x", shape, _mybir.dt.float32, kind="ExternalOutput").ap())
    sandwich(nc, *args)
    return _run(nc, [arrays], core_ids=[0]).results[0]["out_x"]
```

```python
import concourse.bass as bass
from concourse import mybir
from contextlib import ExitStack

P = 128
SEQ = 256
HALF = 4
TILES = 2 * HALF
HW = HALF * P
GW = TILES * P
EPS = 1e-5


def sandwich(nc, x, A_param, B_vec, C_vec, D_vec, W_proj, b_proj, gamma, beta, W_r, W_k, W_v, mu_r, mu_k, out):
    fp32 = mybir.dt.float32
    ALU = mybir.AluOpType
    ACT = mybir.ActivationFunctionType
    AX = mybir.AxisListType.X

    tokens = x.shape[0] * x.shape[1]
    GROUPS = tokens // GW
    LAST = GROUPS - 1
    x_dram = x.rearrange("b l c -> (b l) c").rearrange("(n p) c -> p n c", p=P)
    out_dram = out.rearrange("b l c -> (b l) c").rearrange("(n p) c -> p n c", p=P)

    def column(v):
        return v.rearrange("(p a) -> p a", a=1)

    ctx = ExitStack()
    with ctx:
        def sb(name, *shape):
            return ctx.enter_context(nc.sbuf_tensor(name, [P, *shape], fp32))

        def pb(name):
            return ctx.enter_context(nc.psum_tensor(name, [P, HW], fp32))

        def sem(name):
            return ctx.enter_context(nc.semaphore(name))

        ident = sb("ident", P)
        prefix_ones = sb("prefix_ones", SEQ)
        neg_half = sb("neg_half", TILES)
        eps_tile = sb("eps_tile", TILES)
        a_col = sb("a_col", 1)
        b_col = sb("b_col", 1)
        c_col = sb("c_col", 1)
        d_col = sb("d_col", 1)
        bias_col = sb("bias_col", 1)
        bias_row = sb("bias_row", P)
        gamma_row = sb("gamma_row", P)
        beta_row = sb("beta_row", P)
        mu_rows = sb("mu_rows", 2, P)
        w_rk = sb("w_rk", 2, P)
        w_pv = sb("w_pv", 2, P)
        a_pow = sb("a_pow", 1, 8)
        pow_up = sb("pow_up", SEQ)
        pow_down = sb("pow_down", SEQ)
        pow_token = sb("pow_token", 2, P)
        mixed = sb("mixed", 4, P)
        mixed_T = sb("mixed_T", 4, P)
        pv_T = sb("pv_T", 2, P)
        sums = sb("sums", 8)
        wait_holder = sb("wait_holder", 1)

        x_all = sb("x_all", GROUPS * GW)

        xn = [sb(f"xn{h}", HW) for h in range(2)]
        xn_pow = [sb(f"xn_pow{h}", HW) for h in range(2)]
        xnT = [sb(f"xnT{h}", HW) for h in range(2)]
        conv_scaled = [sb(f"conv_scaled{h}", HW) for h in range(2)]
        conv = [sb(f"conv{h}", HW) for h in range(2)]
        gelu = [sb(f"gelu{h}", HW) for h in range(2)]
        y = [sb(f"y{h}", HW) for h in range(2)]
        ts_ = [sb(f"t_scaled{h}", HW) for h in range(2)]
        tsT = [sb(f"tsT{h}", 2, SEQ + 1) for h in range(2)]
        k_act = [sb(f"k_act{h}", HW) for h in range(2)]
        tanh = [sb(f"tanh{h}", HW) for h in range(2)]
        f = [sb(f"f{h}", HW) for h in range(2)]
        f_normal = [sb(f"f_normal{h}", HW) for h in range(2)]
        junk = sb("junk", GW)

        def stats(name):
            return {"raw": sb(f"{name}_raw", TILES, 6),
                    **{k: sb(f"{name}_{k}", TILES) for k in ("diff", "m2", "sq", "msum", "negmean", "ve", "r")}}

        Sx, Sy, St, Sf = (stats(n) for n in ("sx", "sy", "st", "sf"))
        z_var = sb("z_var", TILES)
        z_ve = sb("z_ve", TILES)
        z_r = sb("z_r", TILES)
        x_bias = sb("x_bias", TILES)
        t_shift = sb("t_shift", GROUPS * TILES)
        f_shift = sb("f_shift", TILES)
        out_bias = sb("out_bias", TILES)

        ps_xT, ps_prefix, ps_z0, ps_z1, ps_tT, ps_k, ps_r, ps_v = (
            pb(n) for n in ("ps_xT", "ps_prefix", "ps_z0", "ps_z1", "ps_tT", "ps_k", "ps_r", "ps_v"))
        ps_z = [ps_z0, ps_z1]

        s_vecs, s_rows, s_wts = sem("vecs_loaded"), sem("rows_loaded"), sem("weights_loaded")
        s_const, s_A, s_pow, s_chain = sem("constants"), sem("A_ready"), sem("powers_ready"), sem("setup_chain")
        s_mixed, s_setupT, s_ready = sem("mixed_ready"), sem("setup_transposed"), sem("weights_ready")
        s_bias, s_filled = sem("bias_ready"), sem("filled")
        s_x0, s_x1, s_xrest = sem("x0_loaded"), sem("x1_loaded"), sem("x_rest_loaded")
        x_stats, x_moments, x_scale = sem("x_stats"), sem("x_moments"), sem("x_scale")
        xn_ready, xn_pow_ready, xT_ready, xT_copied = (sem(n) for n in (
            "xn_ready", "xn_pow_ready", "xT_ready", "xT_copied"))
        prefix_ready, scaled_ready, conv_ready, gelu_ready = (sem(n) for n in (
            "prefix_ready", "scaled_ready", "conv_ready", "gelu_ready"))
        z_ready, y_scaled, y_ready = sem("z_ready"), sem("y_scaled"), sem("y_ready")
        z_squares, z_scale = sem("z_squares"), sem("z_scale")
        y_stats, y_moments, y_scale, t_ready = (sem(n) for n in ("y_stats", "y_moments", "y_scale", "t_ready"))
        t_stats, t_moments, t_scale = sem("t_stats"), sem("t_moments"), sem("t_scale")
        ts_ready, tT_ready, tT_copied = sem("ts_ready"), sem("tT_ready"), sem("tT_copied")
        k_ready, r_ready, relu_done, k_act_ready, tanh_done, v_ready, f_ready = (sem(n) for n in (
            "k_ready", "r_ready", "relu_done", "k_act_ready", "tanh_done", "v_ready", "f_ready"))
        f_stats, f_moments, f_scale = sem("f_stats"), sem("f_moments"), sem("f_scale")
        f_scaled, out_ready = sem("f_scaled"), sem("out_ready")
        stored = sem("stored")
        pc = {n: sem(f"pool_{n}") for n in ("x", "z", "y", "shift", "f", "f_shift")}
        dc = {n: (sem(f"dve_{n}_diff"), sem(f"dve_{n}_sq")) for n in ("x", "y", "t", "f")}

        block = ctx.enter_context(nc.Block())

        def tile(t, j):
            return t[:, j * P:(j + 1) * P]

        def xa(g, j, n=1):
            return x_all[:, bass.ds(g * GW + j * P, n * P)]

        def shift_of(g):
            return t_shift[:, bass.ds(g * TILES, TILES)]

        def runs(g, s):
            return not isinstance(g, int) or 0 <= g - s < GROUPS

        def later(eng, s, value, g):
            if not isinstance(g, int) or value > 0:
                eng.wait_ge(s, value)

        @block.sync
        def _(sp):
            sp.dma_start(x_all[:, 0:GW].rearrange("p (n c) -> p n c", c=P), x_dram[:, 0:TILES, :]).then_inc(s_x0, 16)
            for dst, src in ((mu_rows[:, 0, :], mu_r), (mu_rows[:, 1, :], mu_k), (bias_row[:], b_proj),
                             (gamma_row[:], gamma), (beta_row[:], beta)):
                sp.dma_start(dst, src.partition_broadcast(P)).then_inc(s_rows, 16)
            for i, w in enumerate((W_proj, W_v)):
                sp.dma_start(w_pv[:, i, :], w).then_inc(s_wts, 16)
            for i, w in enumerate((W_r, W_k)):
                sp.dma_start(w_rk[:, i, :], w).then_inc(s_wts, 16)
            sp.dma_start(x_all[:, GW:2 * GW].rearrange("p (n c) -> p n c", c=P),
                         x_dram[:, TILES:2 * TILES, :]).then_inc(s_x1, 16)
            with sp.Fori(2, GROUPS) as g:
                sp.dma_start(x_all[:, bass.ds(g * GW, GW)].rearrange("p (n c) -> p n c", c=P),
                             x_dram[:, bass.ds(g * TILES, TILES), :]).then_inc(s_xrest, 16)
            with sp.Fori(0, GROUPS) as g:
                sp.wait_ge(out_ready, 2 * g + 2)
                sp.dma_start(out_dram[:, bass.ds(g * TILES, TILES), :],
                             x_all[:, bass.ds(g * GW, GW)].rearrange("p (n c) -> p n c", c=P)).then_inc(stored, 16)
            sp.wait_ge(stored, 16 * GROUPS)

        @block.gpsimd
        def _(pool):
            g_ = nc.gpsimd
            g_.memset(ident[:], 0.0).then_inc(s_filled, 1)
            g_.memset(prefix_ones[:], 1.0).then_inc(s_filled, 1)
            g_.memset(neg_half[:], -0.5)
            g_.memset(eps_tile[:], EPS)
            for h in range(2):
                g_.memset(tsT[h][:, :, 0:1], 0.0)
            pool.wait_ge(s_filled, 2)
            g_.affine_select(out=ident[:], in_=ident[:], compare_op=ALU.not_equal, fill=1.0, base=0,
                             pattern=[[-1, P]], channel_multiplier=1)
            g_.affine_select(out=prefix_ones[:], in_=prefix_ones[:], compare_op=ALU.is_ge, fill=0.0, base=0,
                             pattern=[[1, SEQ]], channel_multiplier=-1).then_inc(s_const, 1)

            def inverse_std(s, done, g):
                g_.tensor_tensor(s["r"][:], s["ve"][:], neg_half[:], ALU.pow).then_inc(done, 1)
                g_.tensor_scalar(s["negmean"][:], s["msum"][:], -0.5, None, ALU.mult).then_inc(done, 1)
                pool.wait_ge(done, 2 * g + 2)

            def pre_scale(g):
                pool.wait_ge(x_moments, g + 1)
                later(pool, xn_ready, 2 * g, g)
                inverse_std(Sx, pc["x"], g)
                g_.tensor_tensor(x_bias[:], Sx["negmean"][:], Sx["r"][:], ALU.mult).then_inc(x_scale, 1)

            def xn_times_pow(g, h):
                n = 2 * g + h
                if isinstance(g, int) and n == 0:
                    pool.wait_ge(s_pow, 1)
                pool.wait_ge(xn_ready, n + 1)
                later(pool, prefix_ready, n - 1, g)
                g_.tensor_tensor(xn_pow[h][:].rearrange("p (q l) -> p q l", l=SEQ),
                                 xn[h][:].rearrange("p (q l) -> p q l", l=SEQ),
                                 pow_token[:].rearrange("p j c -> p (j c)")[:, None, :].to_broadcast([P, 2, SEQ]),
                                 ALU.mult).then_inc(xn_pow_ready, 1)

            def z_scale_of(g):
                pool.wait_ge(z_squares, 2 * g + 2)
                later(pool, y_scaled, 2 * g, g)
                g_.tensor_tensor(z_ve[:], z_var[:], eps_tile[:], ALU.add).then_inc(pc["z"], 1)
                pool.wait_ge(pc["z"], g + 1)
                g_.tensor_tensor(z_r[:], z_ve[:], neg_half[:], ALU.pow).then_inc(z_scale, 1)

            def add_beta(g, h):
                if isinstance(g, int) and g == 0:
                    pool.wait_ge(s_rows, 16 * 5)
                pool.wait_ge(y_scaled, 2 * g + h + 1)
                yv = y[h][:].rearrange("p (j c) -> p j c", c=P)
                g_.tensor_tensor(yv, yv, beta_row[:, None, :].to_broadcast([P, HALF, P]), ALU.add).then_inc(y_ready, 1)

            def y_scale_of(g):
                pool.wait_ge(y_moments, g + 1)
                later(pool, pc["shift"], g, g)
                later(pool, t_ready, 2 * g, g)
                g_.tensor_tensor(Sy["r"][:], Sy["ve"][:], neg_half[:], ALU.pow).then_inc(y_scale, 1)
                g_.tensor_scalar(Sy["negmean"][:], Sy["msum"][:], -0.5, None, ALU.mult).then_inc(pc["y"], 1)
                pool.wait_ge(s_const, 1)
                pool.wait_ge(pc["y"], g + 1)
                g_.tensor_tensor(shift_of(g), Sy["negmean"][:], Sy["r"][:], ALU.mult).then_inc(pc["shift"], 1)

            def t_scale_of(g):
                pool.wait_ge(t_moments, g + 1)
                later(pool, ts_ready, 2 * g, g)
                g_.tensor_tensor(St["r"][:], St["ve"][:], neg_half[:], ALU.pow).then_inc(t_scale, 1)

            def f_scale_of(g):
                pool.wait_ge(f_moments, g + 1)
                later(pool, f_scaled, 2 * g, g)
                inverse_std(Sf, pc["f"], g)
                g_.tensor_tensor(f_shift[:], Sf["negmean"][:], Sf["r"][:], ALU.mult).then_inc(pc["f_shift"], 1)
                pool.wait_ge(s_const, 1)
                pool.wait_ge(pc["shift"], g + 1)
                pool.wait_ge(pc["f_shift"], g + 1)
                g_.tensor_tensor(out_bias[:], f_shift[:], shift_of(g), ALU.add).then_inc(f_scale, 1)

            def add_f(g, h):
                pool.wait_ge(s_const, 1)
                pool.wait_ge(f_scaled, 2 * g + h + 1)
                g_.tensor_tensor(xa(g, h * HALF, HALF), f_normal[h][:], xa(g, h * HALF, HALF),
                                 ALU.add).then_inc(out_ready, 1)

            def body(g):
                if runs(g, 2):
                    add_beta(g - 2, 1)
                if runs(g, 5):
                    add_f(g - 5, 0)
                if runs(g, 0):
                    pre_scale(g)
                if runs(g, 5):
                    add_f(g - 5, 1)
                if runs(g, 2):
                    y_scale_of(g - 2)
                if runs(g, 0):
                    xn_times_pow(g, 0)
                if runs(g, 4):
                    f_scale_of(g - 4)
                if runs(g, 1):
                    z_scale_of(g - 1)
                if runs(g, 0):
                    xn_times_pow(g, 1)
                if runs(g, 2):
                    t_scale_of(g - 2)
                if runs(g, 1):
                    add_beta(g - 1, 0)

            pool.wait_ge(s_const, 1)
            DEEP = 5
            for g in range(DEEP + 1):
                body(g)
            with pool.Fori(DEEP + 1, GROUPS) as g:
                body(g)
            for g in range(GROUPS, GROUPS + DEEP):
                body(g)

        @block.scalar
        def _(act):
            a_ = nc.scalar
            for dst, src in ((a_col, A_param), (b_col, B_vec), (c_col, C_vec), (d_col, D_vec), (bias_col, b_proj)):
                act.dma_start(dst[:], column(src)).then_inc(s_vecs, 16)
            act.wait_ge(s_vecs, 16 * 5)
            a_.activation(a_pow[:, 0, 0:1], a_col[:], ACT.Sigmoid).then_inc(s_A, 1)

            def normalise(g, h):
                n = 2 * g + h
                act.wait_ge(x_scale, g + 1)
                later(act, xT_ready, n - 1, g)
                later(act, xn_pow_ready, n - 1, g)
                for j in range(HALF):
                    k = h * HALF + j
                    last = a_.activation(tile(xn[h], j), xa(g, k), ACT.Identity, bias=x_bias[:, k:k + 1],
                                         scale=Sx["r"][:, k:k + 1])
                last.then_inc(xn_ready, 1)

            def copy_xT(g, h):
                n = 2 * g + h
                if isinstance(g, int) and n == 0:
                    act.wait_ge(s_bias, 1)
                act.wait_ge(xT_ready, n + 1)
                later(act, z_ready, n - 1, g)
                a_.activation(xnT[h][:], ps_xT[:], ACT.Identity, bias=bias_col[:]).then_inc(xT_copied, 1)

            def gelu_of(g, h):
                n = 2 * g + h
                act.wait_ge(conv_ready, n + 1)
                later(act, z_ready, n - 1, g)
                a_.activation(gelu[h][:], conv[h][:], ACT.Gelu).then_inc(gelu_ready, 1)

            def square_z(g, h):
                act.wait_ge(z_ready, 2 * g + h + 1)
                later(act, z_scale, g, g)
                for j in range(HALF):
                    k = h * HALF + j
                    last = a_.activation(tile(junk, k), tile(ps_z[h], j), ACT.Square, scale=float(P) ** -0.5,
                                         accum_out=z_var[:, k:k + 1])
                last.then_inc(z_squares, 1)

            def scale_f(g, h):
                act.wait_ge(f_scale, g + 1)
                later(act, out_ready, 2 * g + h - 1, g)
                for j in range(HALF):
                    k = h * HALF + j
                    last = a_.activation(tile(f_normal[h], j), tile(f[h], j), ACT.Identity, bias=out_bias[:, k:k + 1],
                                         scale=Sf["r"][:, k:k + 1])
                last.then_inc(f_scaled, 1)

            def scale_t(g, h):
                act.wait_ge(t_scale, g + 1)
                later(act, tT_ready, 2 * g + h - 1, g)
                for j in range(HALF):
                    k = h * HALF + j
                    last = a_.activation(tile(ts_[h], j), xa(g, k), ACT.Copy, scale=St["r"][:, k:k + 1])
                last.then_inc(ts_ready, 1)

            def copy_tT(g, h):
                n = 2 * g + h
                act.wait_ge(tT_ready, n + 1)
                later(act, r_ready, n - 1, g)
                a_.activation(tsT[h][:, :, 1:SEQ + 1], ps_tT[:].rearrange("p (q l) -> p q l", l=SEQ),
                              ACT.Copy).then_inc(tT_copied, 1)

            def relu_k(g, h):
                n = 2 * g + h
                act.wait_ge(k_ready, n + 1)
                later(act, v_ready, n - 1, g)
                a_.activation(k_act[h][:], ps_k[:], ACT.Relu).then_inc(relu_done, 1)

            def square_k(g, h):
                act.wait_ge(relu_done, 2 * g + h + 1)
                a_.activation(k_act[h][:], k_act[h][:], ACT.Square).then_inc(k_act_ready, 1)

            def tanh_r(g, h):
                n = 2 * g + h
                act.wait_ge(r_ready, n + 1)
                later(act, f_ready, n - 1, g)
                a_.activation(tanh[h][:], ps_r[:], ACT.Tanh, scale=0.5).then_inc(tanh_done, 1)

            def body(g):
                if runs(g, 5):
                    scale_f(g - 5, 1)
                if runs(g, 3):
                    scale_t(g - 3, 0)
                if runs(g, 4):
                    tanh_r(g - 4, 1)
                if runs(g, 1):
                    square_z(g - 1, 0)
                if runs(g, 3):
                    copy_tT(g - 3, 0)
                if runs(g, 3):
                    scale_t(g - 3, 1)
                if runs(g, 0):
                    normalise(g, 0)
                if runs(g, 1):
                    gelu_of(g - 1, 1)
                if runs(g, 0):
                    normalise(g, 1)
                if runs(g, 3):
                    copy_tT(g - 3, 1)
                if runs(g, 1):
                    square_z(g - 1, 1)
                if runs(g, 0):
                    copy_xT(g, 0)
                if runs(g, 3):
                    relu_k(g - 3, 0)
                if runs(g, 3):
                    square_k(g - 3, 0)
                if runs(g, 3):
                    tanh_r(g - 3, 0)
                if runs(g, 4):
                    scale_f(g - 4, 0)
                if runs(g, 0):
                    gelu_of(g, 0)
                if runs(g, 0):
                    copy_xT(g, 1)
                if runs(g, 3):
                    relu_k(g - 3, 1)
                if runs(g, 3):
                    square_k(g - 3, 1)

            DEEP = 5
            for g in range(DEEP + 1):
                body(g)
            with act.Fori(DEEP + 1, GROUPS) as g:
                body(g)
            for g in range(GROUPS, GROUPS + DEEP):
                body(g)

        @block.vector
        def _(dve):
            v_ = nc.vector
            link_count = [0]

            def link(ins):
                link_count[0] += 1
                ins.then_inc(s_chain, 1)
                dve.wait_ge(s_chain, link_count[0])

            def moments(s, name, g, h, source, stats_done, moments_done, used, eps=EPS):
                for j in range(HALF):
                    last = v_.bn_stats(s["raw"][:, h * HALF + j, :], source(j))
                if h == 1:
                    last.then_inc(stats_done, 1)
                    join(s, name, g, stats_done, moments_done, used, eps)

            def join(s, name, g, stats_done, moments_done, used, eps):
                even_mean, even_m2, odd_mean, odd_m2 = (s["raw"][:, :, c] for c in (1, 2, 4, 5))
                dve.wait_ge(stats_done, g + 1)
                later(dve, used, g, g)
                v_.tensor_tensor(s["diff"][:], even_mean, odd_mean, ALU.subtract).then_inc(dc[name][0], 1)
                v_.tensor_tensor(s["msum"][:], even_mean, odd_mean, ALU.add)
                v_.scalar_tensor_tensor(s["m2"][:], even_m2, P * eps, odd_m2, ALU.add, ALU.add)
                dve.wait_ge(dc[name][0], g + 1)
                v_.scalar_tensor_tensor(s["sq"][:], s["diff"][:], 0.25, s["diff"][:], ALU.mult,
                                        ALU.mult).then_inc(dc[name][1], 1)
                dve.wait_ge(dc[name][1], g + 1)
                v_.scalar_tensor_tensor(s["ve"][:], s["m2"][:], 1.0 / P, s["sq"][:], ALU.mult,
                                        ALU.add).then_inc(moments_done, 1)

            def x_moments_of(g, h):
                if isinstance(g, int) and g < 2:
                    dve.wait_ge((s_x0, s_x1)[g], 16)
                else:
                    dve.wait_ge(s_xrest, 16 * (GROUPS - 2))
                moments(Sx, "x", g, h, lambda j: xa(g, h * HALF + j), x_stats, x_moments, x_scale)

            def y_moments_of(g, h):
                dve.wait_ge(y_ready, 2 * g + h + 1)
                moments(Sy, "y", g, h, lambda j: tile(y[h], j), y_stats, y_moments, pc["shift"])

            def t_moments_of(g, h):
                dve.wait_ge(t_ready, 2 * g + h + 1)
                v_.tensor_tensor(wait_holder[:], d_col[:], d_col[:], ALU.mult)
                moments(St, "t", g, h, lambda j: xa(g, h * HALF + j), t_stats, t_moments, t_scale)

            def convolve(g, h):
                n = 2 * g + h
                dve.wait_ge(prefix_ready, n + 1)
                v_.tensor_tensor(conv_scaled[h][:].rearrange("p (q l) -> p q l", l=SEQ),
                                 ps_prefix[:].rearrange("p (q l) -> p q l", l=SEQ),
                                 pow_down[:, None, :].to_broadcast([P, 2, SEQ]), ALU.mult).then_inc(scaled_ready, 1)
                dve.wait_ge(scaled_ready, n + 1)
                dve.wait_ge(xT_copied, n + 1)
                later(dve, gelu_ready, n - 1, g)
                v_.scalar_tensor_tensor(conv[h][:], ps_xT[:], d_col[:], conv_scaled[h][:], ALU.mult,
                                        ALU.add).then_inc(conv_ready, 1)

            def scale_z(g, h):
                dve.wait_ge(z_scale, g + 1)
                later(dve, t_ready, 2 * g + h - 1, g)
                for j in range(HALF):
                    k = h * HALF + j
                    last = v_.scalar_tensor_tensor(tile(y[h], j), tile(ps_z[h], j), z_r[:, k:k + 1], gamma_row[:],
                                                   ALU.mult, ALU.mult)
                last.then_inc(y_scaled, 1)

            def residual(g, h):
                dve.wait_ge(y_scale, g + 1)
                for j in range(HALF):
                    k = h * HALF + j
                    last = v_.scalar_tensor_tensor(xa(g, k), tile(y[h], j), Sy["r"][:, k:k + 1], xa(g, k),
                                                   ALU.mult, ALU.add)
                last.then_inc(t_ready, 1)

            def gate(g, h):
                n = 2 * g + h
                later(dve, f_scaled, n - 1, g)
                dve.wait_ge(tanh_done, n + 1)
                dve.wait_ge(v_ready, n + 1)
                v_.scalar_tensor_tensor(f[h][:], tanh[h][:], 1.0, ps_v[:], ALU.add, ALU.mult).then_inc(f_ready, 1)
                dve.wait_ge(f_ready, n + 1)
                moments(Sf, "f", g, h, lambda j: tile(f[h], j), f_stats, f_moments, f_scale, 4 * EPS)

            def body(g):
                if runs(g, 0) and not (isinstance(g, int) and g == 0):
                    x_moments_of(g, 0)
                if runs(g, 3):
                    residual(g - 3, 0)
                if runs(g, 3):
                    t_moments_of(g - 3, 0)
                if runs(g, 3):
                    residual(g - 3, 1)
                if runs(g, 3):
                    t_moments_of(g - 3, 1)
                if runs(g, 1):
                    convolve(g - 1, 0)
                if runs(g, 2):
                    scale_z(g - 2, 0)
                if runs(g, 2):
                    scale_z(g - 2, 1)
                if runs(g, 0) and not (isinstance(g, int) and g == 0):
                    x_moments_of(g, 1)
                if runs(g, 4):
                    gate(g - 4, 0)
                if runs(g, 2):
                    y_moments_of(g - 2, 0)
                if runs(g, 2):
                    y_moments_of(g - 2, 1)
                if runs(g, 1):
                    convolve(g - 1, 1)
                if runs(g, 4):
                    gate(g - 4, 1)

            x_moments_of(0, 0)
            x_moments_of(0, 1)
            dve.wait_ge(s_vecs, 16 * 5)
            v_.memset(pow_up[:, 0:1], 1.0)
            link(v_.tensor_tensor(pow_down[:, SEQ - 1:SEQ], c_col[:], b_col[:], ALU.mult))
            dve.wait_ge(s_A, 1)
            for k in range(8):
                n = 1 << k
                power = a_pow[:, 0, k:k + 1]
                v_.tensor_scalar(pow_up[:, n:2 * n], pow_up[:, 0:n], power, None, ALU.mult)
                step = v_.tensor_scalar(pow_down[:, SEQ - 2 * n:SEQ - n], pow_down[:, SEQ - n:SEQ], power, None,
                                        ALU.mult)
                if k < 7:
                    step = v_.tensor_tensor(a_pow[:, 0, k + 1:k + 2], power, power, ALU.mult)
                link(step)
            v_.tensor_copy(sums[:, 7:8], pow_up[:, 0:1]).then_inc(s_mixed, 1)
            dve.wait_ge(s_setupT, 1)
            v_.tensor_copy(pow_token[:].rearrange("p j c -> p (j c)"), ps_v[:, 0:SEQ]).then_inc(s_pow, 1)
            dve.wait_ge(s_rows, 16 * 5)
            link(v_.reduce_sum(sums[:, 4:5], bias_row[:], axis=AX))
            link(v_.tensor_scalar(sums[:, 5:6], sums[:, 4:5], 1.0 / P, None, ALU.mult))
            v_.tensor_scalar(bias_col[:], bias_col[:], sums[:, 5:6], None, ALU.subtract).then_inc(s_bias, 1)
            dve.wait_ge(s_setupT, 2)
            link(v_.reduce_sum(sums[:, 4:5], ps_k[:, 0:P], axis=AX))
            link(v_.tensor_scalar(sums[:, 5:6], sums[:, 4:5], 1.0 / P, None, ALU.mult))
            v_.tensor_scalar(pv_T[:, 0, :], ps_k[:, 0:P], sums[:, 5:6], None, ALU.subtract)
            v_.tensor_copy(pv_T[:, 1, :], ps_k[:, P:2 * P]).then_inc(s_ready, 1)
            dve.wait_ge(s_wts, 16 * 4)
            mixed_pairs = mixed[:].rearrange("p (w m) c -> p w m c", m=2)
            link(v_.tensor_tensor(mixed_pairs[:, :, 0, :], w_rk[:], mu_rows[:], ALU.mult))
            link(v_.tensor_tensor(mixed_pairs[:, :, 1, :], w_rk[:], mixed_pairs[:, :, 0, :], ALU.subtract))
            link(v_.reduce_sum(sums[:, 0:4], mixed[:], axis=AX))
            link(v_.tensor_scalar(sums[:, 0:4], sums[:, 0:4], 1.0 / P, None, ALU.mult))
            v_.tensor_tensor(mixed[:], mixed[:], sums[:, 0:4, None].to_broadcast([P, 4, P]),
                             ALU.subtract).then_inc(s_mixed, 1)
            dve.wait_ge(s_setupT, 3)
            v_.tensor_copy(mixed_T[:].rearrange("p w c -> p (w c)"), ps_r[:]).then_inc(s_ready, 1)

            DEEP = 4
            for g in range(DEEP + 1):
                body(g)
            with dve.Fori(DEEP + 1, GROUPS) as g:
                body(g)
            for g in range(GROUPS, GROUPS + DEEP):
                body(g)

        @block.tensor
        def _(pe):
            t_ = nc.tensor
            pe.wait_ge(s_const, 1)
            pe.wait_ge(s_mixed, 1)
            for j in range(2):
                last = t_.transpose(ps_v[:, j * P:(j + 1) * P], pow_up[:, j * P:(j + 1) * P], ident[:])
            last.then_inc(s_setupT, 1)
            pe.wait_ge(s_wts, 16 * 4)
            for j in range(2):
                last = t_.transpose(ps_k[:, j * P:(j + 1) * P], w_pv[:, j, :], ident[:])
            last.then_inc(s_setupT, 1)

            def transpose_mixed():
                pe.wait_ge(s_mixed, 2)
                for j in range(4):
                    last = t_.transpose(ps_r[:, j * P:(j + 1) * P], mixed[:, j, :], ident[:])
                last.then_inc(s_setupT, 1)

            def transpose_xn(g, h):
                n = 2 * g + h
                pe.wait_ge(xn_ready, n + 1)
                later(pe, conv_ready, n, g)
                for j in range(HALF):
                    last = t_.transpose(tile(ps_xT, j), tile(xn[h], j), ident[:])
                last.then_inc(xT_ready, 1)

            def prefix_sum(g, h):
                n = 2 * g + h
                pe.wait_ge(xn_pow_ready, n + 1)
                later(pe, scaled_ready, n, g)
                for q in range(2):
                    t_.matmul(ps_prefix[:, q * SEQ:(q + 1) * SEQ], tile(xn_pow[h], 2 * q), prefix_ones[:],
                              start=True, stop=False)
                    last = t_.matmul(ps_prefix[:, q * SEQ + P:(q + 1) * SEQ], tile(xn_pow[h], 2 * q + 1),
                                     prefix_ones[:, 0:P], start=False, stop=True)
                last.then_inc(prefix_ready, 1)
                if isinstance(g, int) and n == 0:
                    transpose_mixed()

            def project(g, h):
                n = 2 * g + h
                if isinstance(g, int) and n == 0:
                    pe.wait_ge(s_ready, 1)
                pe.wait_ge(gelu_ready, n + 1)
                pe.wait_ge(xT_copied, n + 1)
                later(pe, y_scaled, n - 1, g)
                for j in range(HALF):
                    t_.matmul(tile(ps_z[h], j), tile(gelu[h], j), pv_T[:, 0, :], start=True, stop=False)
                    last = t_.matmul(tile(ps_z[h], j), tile(xnT[h], j), ident[:], is_transpose=True,
                                     start=False, stop=True)
                last.then_inc(z_ready, 1)

            def transpose_t(g, h):
                n = 2 * g + h
                pe.wait_ge(ts_ready, n + 1)
                later(pe, tT_copied, n, g)
                for j in range(HALF):
                    last = t_.transpose(tile(ps_tT, j), tile(ts_[h], j), ident[:])
                last.then_inc(tT_ready, 1)

            def keys(g, h):
                n = 2 * g + h
                if isinstance(g, int) and n == 0:
                    pe.wait_ge(s_ready, 2)
                pe.wait_ge(tT_copied, n + 1)
                later(pe, relu_done, n, g)
                k_out = ps_k[:].rearrange("p (q l) -> p q l", l=SEQ)
                t_.matmul(k_out, mixed_T[:, 2, :], tsT[h][:, :, 1:SEQ + 1], start=True, stop=False)
                t_.matmul(k_out, mixed_T[:, 3, :], tsT[h][:, :, 0:SEQ], start=False, stop=True).then_inc(k_ready, 1)

            def gates(g, h):
                n = 2 * g + h
                if isinstance(g, int) and n == 0:
                    pe.wait_ge(s_ready, 2)
                later(pe, tanh_done, n, g)
                for j in range(HALF):
                    q, l = j // 2, (j % 2) * P
                    t_.matmul(tile(ps_r, j), tsT[h][:, q, l + 1:l + 1 + P], mixed_T[:, 0, :], start=True, stop=False)
                    last = t_.matmul(tile(ps_r, j), tsT[h][:, q, l:l + P], mixed_T[:, 1, :], start=False, stop=True)
                last.then_inc(r_ready, 1)

            def values(g, h):
                n = 2 * g + h
                pe.wait_ge(k_act_ready, n + 1)
                later(pe, f_ready, n, g)
                for j in range(HALF):
                    last = t_.matmul(tile(ps_v, j), tile(k_act[h], j), pv_T[:, 1, :], start=True, stop=True)
                last.then_inc(v_ready, 1)

            def body(g):
                if runs(g, 1):
                    prefix_sum(g - 1, 1)
                if runs(g, 4):
                    values(g - 4, 1)
                if runs(g, 3):
                    transpose_t(g - 3, 0)
                if runs(g, 3):
                    keys(g - 3, 0)
                if runs(g, 3):
                    transpose_t(g - 3, 1)
                if runs(g, 0):
                    transpose_xn(g, 0)
                if runs(g, 1):
                    project(g - 1, 1)
                if runs(g, 3):
                    gates(g - 3, 0)
                if runs(g, 0):
                    prefix_sum(g, 0)
                if runs(g, 3):
                    keys(g - 3, 1)
                if runs(g, 3):
                    values(g - 3, 0)
                if runs(g, 0):
                    transpose_xn(g, 1)
                if runs(g, 3):
                    gates(g - 3, 1)
                if runs(g, 0):
                    project(g, 0)

            DEEP = 4
            for g in range(DEEP + 1):
                body(g)
            with pe.Fori(DEEP + 1, GROUPS) as g:
                body(g)
            for g in range(GROUPS, GROUPS + DEEP):
                body(g)


_INS = ["x", "A_param", "B_vec", "C_vec", "D_vec", "W_proj", "b_proj", "gamma", "beta",
        "W_r", "W_k", "W_v", "mu_r", "mu_k"]


def kernel(**inputs):
    import numpy as _np
    import concourse.bacc as _bacc
    from concourse import mybir as _mybir
    from concourse.bass_utils import run_bass_kernel_spmd as _run

    nc = _bacc.Bacc("TRN2", target_bir_lowering=False, num_devices=1)
    arrays, args = {}, []
    for i, name in enumerate(_INS):
        a = _np.ascontiguousarray(inputs[("L0_attn_" if i < 9 else "L0_ffn_") + name])
        arrays[f"in_{name}"] = a
        args.append(nc.dram_tensor(f"in_{name}", a.shape, _mybir.dt.from_np(a.dtype), kind="ExternalInput").ap())
    shape = inputs["L0_attn_x"].shape
    args.append(nc.dram_tensor("out_x", shape, _mybir.dt.float32, kind="ExternalOutput").ap())
    sandwich(nc, *args)
    return _run(nc, [arrays], core_ids=[0]).results[0]["out_x"]
```
